# Optimizing a Trainium2 kernel written in Bass

```python
import numpy as np
import jax
import jax.numpy as jnp

def _softmax(x, axis=-1):
    return jax.nn.softmax(x, axis=axis)

def _gelu(x):
    return jax.nn.gelu(x, approximate=True)

def _silu(x):
    return jax.nn.silu(x)

def _sigmoid(x):
    return jax.nn.sigmoid(x)

def _layernorm(x, axis=-1, eps=1e-05):
    m = jnp.mean(x, axis=axis, keepdims=True)
    v = jnp.var(x, axis=axis, keepdims=True)
    return (x - m) / jnp.sqrt(v + eps)

def _scatter_add(tgt, idx, src, axis=0):
    return tgt.at[idx].add(src)

def _segment_sum(src, seg, n):
    return jax.ops.segment_sum(src, seg, n)
kernel_name = 'mk_gnn_resnorm_d2_gnn_r8_771559'

def setup_inputs(seed: int=0):
    np.random.seed(seed)
    _w = jnp.asarray

    def _rec_inputs():
        import jax
        import jax.numpy as jnp
        _gk = jax.random.key(seed)
        x = -0.0003713 + 1 * jax.random.normal(jax.random.fold_in(_gk, 1), (12500, 128), jnp.float32)
        _s = jax.random.randint(jax.random.fold_in(_gk, 2), (100000,), 0, 12500, jnp.int32)
        _d = jax.random.randint(jax.random.fold_in(_gk, 3), (100000,), 0, 12500, jnp.int32)
        _loop = jnp.arange(12500, dtype=jnp.int32)
        src = jnp.concatenate([_s, _d, _loop])
        dst = jnp.concatenate([_d, _s, _loop])
        _o = jnp.argsort(dst, stable=True)
        src = src[_o]
        dst = dst[_o]
        edge_type_16 = jax.random.randint(jax.random.fold_in(_gk, 12), (212500,), 0, 16, jnp.int32)
        return (x, src, dst, edge_type_16)
    x, src, dst, edge_type_16 = _rec_inputs()

    def _L0_gnn_setup():
        import jax, jax.numpy as jnp
        import numpy as np
        N_NODES = 12500
        N_EDGES = 400000
        IN_FEAT = 128
        OUT_FEAT = 128
        NUM_RELS = 16
        NUM_BASES = 8
        key = jax.random.key(seed)
        ks = jax.random.split(key, 7)
        x = jax.random.normal(ks[0], (N_NODES, IN_FEAT), dtype=jnp.float32)
        src = jax.random.randint(ks[1], (N_EDGES,), 0, N_NODES, dtype=jnp.int64)
        dst = jax.random.randint(ks[2], (N_EDGES,), 0, N_NODES, dtype=jnp.int64)
        etypes = jax.random.randint(ks[3], (N_EDGES,), 0, NUM_RELS, dtype=jnp.int64)
        gain = float(np.sqrt(2.0))
        limit_w = gain * float(np.sqrt(6.0 / (IN_FEAT + OUT_FEAT)))
        weight = jax.random.uniform(ks[4], (NUM_BASES, IN_FEAT, OUT_FEAT), dtype=jnp.float32, minval=-limit_w, maxval=limit_w)
        limit_c = float(np.sqrt(6.0 / (NUM_RELS + NUM_BASES)))
        w_comp = jax.random.uniform(ks[5], (NUM_RELS, NUM_BASES), dtype=jnp.float32, minval=-limit_c, maxval=limit_c)
        h_bias = jnp.zeros((OUT_FEAT,), dtype=jnp.float32)
        return {'x': x, 'weight': weight, 'w_comp': w_comp, 'h_bias': h_bias, 'src': src, 'dst': dst, 'etypes': etypes}
    _L0_gnn_all = _L0_gnn_setup()
    _L0_gnn_in = {k: v for k, v in _L0_gnn_all.items() if k in ('weight', 'w_comp', 'h_bias')}
    del _L0_gnn_all

    def _L1_gnn_setup():
        import jax, jax.numpy as jnp
        import numpy as np
        N_NODES = 12500
        N_EDGES = 200000
        D_IN = 128
        D_OUT = 128
        key = jax.random.key(seed)
        k1, k2, k3, k4, k5 = jax.random.split(key, 5)
        feat = jax.random.normal(k1, (N_NODES, D_IN), dtype=jnp.float32)
        W_neigh = jax.random.normal(k2, (D_IN, D_OUT), dtype=jnp.float32) * (1.0 / np.sqrt(D_IN))
        W_self = jax.random.normal(k3, (D_IN, D_OUT), dtype=jnp.float32) * (1.0 / np.sqrt(D_IN))
        b_self = jnp.zeros((D_OUT,), dtype=jnp.float32)
        src = jax.random.randint(k4, (N_EDGES,), 0, N_NODES, dtype=jnp.int32)
        dst = jnp.sort(jax.random.randint(k5, (N_EDGES,), 0, N_NODES, dtype=jnp.int32))
        return {'feat': feat, 'W_neigh': W_neigh, 'W_self': W_self, 'b_self': b_self, 'src': src, 'dst': dst}
    _L1_gnn_all = _L1_gnn_setup()
    _L1_gnn_in = {k: v for k, v in _L1_gnn_all.items() if k in ('W_neigh', 'W_self', 'b_self')}
    del _L1_gnn_all
    return {'x': x, 'src': src, 'dst': dst, 'edge_type_16': edge_type_16, 'L0_gnn_weight': _L0_gnn_in['weight'], 'L0_gnn_w_comp': _L0_gnn_in['w_comp'], 'L0_gnn_h_bias': _L0_gnn_in['h_bias'], 'L1_gnn_W_neigh': _L1_gnn_in['W_neigh'], 'L1_gnn_W_self': _L1_gnn_in['W_self'], 'L1_gnn_b_self': _L1_gnn_in['b_self']}

def reference(x, src, dst, edge_type_16, L0_gnn_weight, L0_gnn_w_comp, L0_gnn_h_bias, L1_gnn_W_neigh, L1_gnn_W_self, L1_gnn_b_self):
    import jax
    import jax.numpy as jnp

    def _L0_gnn_ref(x, weight, w_comp, h_bias, src, dst, etypes):
        import jax, jax.numpy as jnp
        import numpy as np
        N_NODES = 12500
        N_EDGES = 400000
        IN_FEAT = 128
        OUT_FEAT = 128
        NUM_RELS = 16
        NUM_BASES = 8
        W = jnp.einsum('rb,bio->rio', w_comp, weight)
        h = jnp.einsum('ni,rio->rno', x, W)
        msg = h[etypes, src]
        node_repr = jax.ops.segment_sum(msg, dst, num_segments=N_NODES)
        node_repr = node_repr + h_bias
        return node_repr

    def _L1_gnn_ref(feat, W_neigh, W_self, b_self, src, dst):
        import jax, jax.numpy as jnp
        import numpy as np
        N_NODES = 12500
        N_EDGES = 200000
        D_IN = 128
        D_OUT = 128
        "SAGE 'mean' aggregation: h = fc_self(feat) + fc_neigh(mean_{u in N(v)} feat_u).\n            in_feats == out_feats -> lin_before_mp is False: aggregate raw features first.\n            In-degrees are clamped to min 1.0 as in set_graph_data."
        n = feat.shape[0]
        deg = jax.ops.segment_sum(jnp.ones_like(dst, dtype=feat.dtype), dst, num_segments=n)
        deg = jnp.maximum(deg, 1.0)
        agg = jax.ops.segment_sum(feat[src], dst, num_segments=n)
        h_neigh = agg / deg[:, None] @ W_neigh
        h_self = feat @ W_self + b_self
        return h_self + h_neigh
    x = _layernorm(x + _L0_gnn_ref(x, L0_gnn_weight, L0_gnn_w_comp, L0_gnn_h_bias, src, dst, edge_type_16), axis=-1)
    x = _layernorm(x + _L1_gnn_ref(x, L1_gnn_W_neigh, L1_gnn_W_self, L1_gnn_b_self, src, dst), axis=-1)
    return x

_drawn_inputs = setup_inputs


def setup_inputs(seed=0):
    import zlib

    import numpy as np

    out = dict(_drawn_inputs(seed))
    spreads = {'L0_gnn_h_bias': (0.0, 0.322), 'L1_gnn_b_self': (0.0, 0.1)}
    factors = {}
    for name, (base, spread) in spreads.items():
        noise = np.random.default_rng([zlib.crc32(name.encode()), seed]).standard_normal(out[name].shape)
        drawn = base * np.exp(spread * noise) if base else spread * noise
        out[name] = jnp.asarray(drawn.astype(out[name].dtype))
    for name, factor in factors.items():
        out[name] = (out[name] * factor).astype(out[name].dtype)
    return out
```

```python
import concourse.bass as bass
from concourse import mybir
from contextlib import ExitStack

F32 = mybir.dt.float32
I32 = mybir.dt.int32
ALU = mybir.AluOpType
ACT = mybir.ActivationFunctionType
AX = mybir.AxisListType.X
DVE_ONLY = [mybir.EngineType.DVE]

P = 128
WIN = 16
CPG = 8
UNROLL = 8
SLOTS = 4
TPH = 4
FAR = 65536.0
EPS = 1e-5


def gnn_kernel(nc, x_in, src, dst, etype, weight, w_comp, h_bias, w_neigh, w_self, b_self, x1_rows, out):
    n_nodes, d = x_in.shape
    (n_edges,) = src.shape
    n_bases = weight.shape[0]
    n_rels = w_comp.shape[0]
    assert d == P and n_rels * CPG == P and weight.shape[1] == d and weight.shape[2] == d

    group_edges = CPG * P
    full_chunks = n_edges // P
    rest_edges = n_edges - full_chunks * P
    etiles = -(-n_edges // (P * P))
    chunks = etiles * P
    groups = chunks // CPG
    bodies = groups // UNROLL
    last_tile_chunks = full_chunks - (etiles - 1) * P
    assert 0 < last_tile_chunks < P and rest_edges > 0 and groups % UNROLL == 0
    last_group = groups - 1
    last_group_chunks = full_chunks - last_group * CPG
    assert 0 < last_group_chunks < CPG

    ntiles = -(-n_nodes // P)
    full_ntiles = n_nodes // P
    rest_nodes = n_nodes - full_ntiles * P
    tiles_p = -(-ntiles // UNROLL) * UNROLL
    nodes_p = tiles_p * P
    nbodies = tiles_p // UNROLL
    assert nodes_p >= n_nodes + WIN and rest_nodes > 0 and tiles_p == TPH * bodies
    GW = CPG * WIN
    HALF = UNROLL // 2

    ctx = ExitStack()
    with ctx:
        def sb(name, shape, dt=F32):
            return ctx.enter_context(nc.sbuf_tensor(name, shape, dt))

        def pb(name, shape):
            return ctx.enter_context(nc.psum_tensor(name, shape, F32))

        def sem(name):
            return ctx.enter_context(nc.semaphore(name))

        acc = sb("acc", [P, 2, nodes_p])
        nodes = sb("nodes", [P, tiles_p, d])
        rows = sb("rows", [P, SLOTS, CPG, d])
        idx = sb("idx", [P, SLOTS, CPG], I32)
        src_t = sb("src_t", [P, chunks + SLOTS * CPG], I32)
        rel_t = sb("rel_t", [P, chunks])
        base = sb("base", [1, chunks], I32)
        span = sb("span", [1, 1], I32)
        ident = sb("ident", [P, P])
        onesm = sb("onesm", [P, P])
        lane_i = sb("lane_i", [P, WIN], I32)
        lane = sb("lane", [P, WIN])
        rel_of_p_i = sb("rel_of_p_i", [P, 1], I32)
        rel_of_p = sb("rel_of_p", [P, 1])
        wc_blk = sb("wc_blk", [P, CPG, n_bases])
        gate = sb("gate", [P, 1])
        bias_col = sb("bias_col", [P, 1])
        bself = sb("bself", [1, d])
        wn = sb("wn", [P, d])
        ws = sb("ws", [P, d])
        stage = sb("stage", [P, 2, TPH, P])
        xt = sb("xt", [P, TPH, P])
        deg_st = sb("deg_st", [1, 2, TPH, P])
        stats = sb("stats", [P, 2, TPH, 6])
        mv = sb("mv", [P, 2, TPH, 2])
        std = sb("std", [P, 2, TPH])
        rstd = sb("rstd", [P, 2, TPH])
        shift = sb("shift", [P, 2, TPH])
        rdeg = sb("rdeg", [P, 2, TPH])
        epst = sb("epst", [P, 1])
        zero = sb("zero", [P, 1])
        oh1 = sb("oh1", [P, 2, CPG, WIN])

        taken = [0]

        def first_layer(words):
            taken[0] += words
            assert taken[0] <= nodes_p
            return acc[:, 1, taken[0] - words:taken[0]]

        a = first_layer(2 * CPG * n_bases * WIN).rearrange("p (u c b n) -> p u c b n", u=2, c=CPG, b=n_bases)
        zsb = first_layer(2 * CPG * n_bases * WIN).rearrange("p (u c b n) -> p u c b n", u=2, c=CPG, b=n_bases)
        eoh = first_layer(2 * HALF * P).rearrange("p (h q e) -> p h q e", h=2, q=HALF)
        erep = first_layer(2 * HALF * P).rearrange("p (h q e) -> p h q e", h=2, q=HALF).bitcast(I32)
        wb = first_layer(n_bases * d).rearrange("p (b o) -> p b o", b=n_bases)
        work0 = first_layer(chunks).rearrange("p (t e) -> p t e", t=etiles)
        work1 = first_layer(chunks).rearrange("p (t e) -> p t e", t=etiles)
        base0 = first_layer(chunks).bitcast(I32)
        src_i = rows[:, 0:2].rearrange("p s c e -> p (s c e)")[:, 0:chunks].rearrange("p (t e) -> p t e", t=etiles).bitcast(I32)
        dst_i = rows[:, 2:4].rearrange("p s c e -> p (s c e)")[:, 0:chunks].rearrange("p (t e) -> p t e", t=etiles).bitcast(I32)
        lo = stats[:, 0, :, :].rearrange("p a b -> p (a b)")[:, 0:etiles]
        hi = stats[:, 1, :, :].rearrange("p a b -> p (a b)")[:, 0:etiles]
        wide = mv[:, 0, 0, 0:1]

        zps = [pb(f"zps{i}", [P, CPG, n_bases, WIN]) for i in range(2)]
        yps = [pb(f"yps{i}", [P, 2, 2, CPG, WIN])[:, 0] for i in range(2)]
        tps = [pb(f"tps{i}", [P, TPH, P]) for i in range(2)]
        wcp = [t[:, :, 0:CPG * n_bases] for t in tps]

        s_pad = sem("s_pad")
        s_ids = sem("s_ids")
        s_w = sem("s_w")
        s_x = sem("s_x")
        s_const = sem("s_const")
        s_blk0 = sem("s_blk0")
        s_bias = sem("s_bias")
        s_pl = sem("s_pl")
        s_dl = sem("s_dl")
        s_al = sem("s_al")
        s_srcf = sem("s_srcf")
        s_relf = sem("s_relf")
        s_lo = sem("s_lo")
        s_tr = sem("s_tr")
        s_trc = sem("s_trc")
        s_rowp = sem("s_rowp")
        quads = [(q, min(TPH, etiles - q)) for q in range(0, etiles, TPH)]

        with nc.Block() as block:
            @block.sync
            def _(sp):
                sp.wait_ge(s_pad, 3)
                for dram, tile in ((dst, dst_i), (src, src_i)):
                    sp.dma_start(tile[:, 0:etiles - 1, :],
                                 dram[0:(etiles - 1) * P * P].rearrange("(t p e) -> p t e", p=P, e=P)).then_inc(s_ids, 16)
                    sp.dma_start(tile[0:last_tile_chunks, etiles - 1, :],
                                 dram[(etiles - 1) * P * P:full_chunks * P].rearrange("(p e) -> p e", e=P)).then_inc(s_ids, 16)
                    sp.dma_start(tile[last_tile_chunks:last_tile_chunks + 1, etiles - 1, 0:rest_edges],
                                 dram[full_chunks * P:n_edges].rearrange("(p e) -> p e", p=1)).then_inc(s_ids, 16)
                sp.dma_start(bias_col[:, :], h_bias.rearrange("(p o) -> p o", o=1)).then_inc(s_bias, 16)
                sp.dma_start(wb, weight.rearrange("b i o -> i b o")).then_inc(s_w, 16)
                sp.dma_start(wn[:, :], w_neigh).then_inc(s_w, 16)
                sp.dma_start(ws[:, :], w_self).then_inc(s_w, 16)
                sp.dma_start(bself[0:1, :], b_self.rearrange("(p o) -> p o", p=1)).then_inc(s_w, 16)
                sp.wait_ge(s_blk0, 1)
                for c in range(CPG):
                    sp.dma_start(wc_blk[c * n_rels:(c + 1) * n_rels, c, :], w_comp).then_inc(s_w, 16)
                sp.dma_start(nodes[0:rest_nodes, full_ntiles, :], x_in[full_ntiles * P:n_nodes, :]).then_inc(s_x, 16)
                sp.dma_start(nodes[:, 0:full_ntiles, :],
                             x_in[0:full_ntiles * P, :].rearrange("(t p) f -> p t f", p=P)).then_inc(s_x, 16)

            @block.gpsimd
            def _(pool):
                nc.gpsimd.iota(lane_i[:, :], pattern=[[1, WIN]], base=0, channel_multiplier=0).then_inc(s_const, 1)
                nc.gpsimd.iota(rel_of_p_i[:, :], pattern=[[0, 1]], base=0, channel_multiplier=1).then_inc(s_const, 1)
                nc.gpsimd.memset(ident[:, :], 0.0).then_inc(s_pl, 1)
                pool.wait_ge(s_pl, 1)
                nc.gpsimd.affine_select(out=ident[:, :], in_=ident[:, :], compare_op=ALU.not_equal, fill=1.0, base=0,
                                        pattern=[[-1, P]], channel_multiplier=1).then_inc(s_const, 1)
                nc.gpsimd.memset(wc_blk[:, :, :], 0.0).then_inc(s_blk0, 1)
                nc.gpsimd.memset(src_t[:, chunks:chunks + SLOTS * CPG], 0)
                nc.gpsimd.memset(erep, 0).then_inc(s_const, 1)

            @block.scalar
            def _(act):
                act.wait_ge(s_ids, 96)
                nc.scalar.copy(work0, src_i).then_inc(s_srcf, 1)
                act.wait_ge(s_bias, 16)
                nc.scalar.copy(acc[:, 0, :], bias_col[:, 0:1].to_broadcast([P, nodes_p])).then_inc(s_al, 1)
                for k, (q, m) in enumerate(quads):
                    act.wait_ge(s_tr, 2 * k + 1)
                    nc.scalar.copy(src_t[:, q * P:(q + m) * P], tps[0][:, 0:m, :]).then_inc(s_trc, 1)
                act.wait_ge(s_al, 1)

            @block.vector
            def _(dve):
                nc.vector.memset(dst_i[:, etiles - 1, :], int(FAR)).then_inc(s_pad, 1)
                nc.vector.memset(src_i[:, etiles - 1, :], 0).then_inc(s_pad, 1)
                nc.vector.memset(nodes[:, full_ntiles:tiles_p, :], 0.0).then_inc(s_pad, 1)
                nc.vector.memset(onesm[:, :], 1.0)
                nc.vector.memset(gate[:, :], 1.0)
                nc.vector.memset(epst[:, :], EPS)
                nc.vector.memset(zero[:, :], 0.0)
                dve.wait_ge(s_const, 4)
                nc.vector.tensor_copy(lane[:, :], lane_i[:, :])
                nc.vector.tensor_scalar(rel_of_p_i[:, :], rel_of_p_i[:, :], n_rels - 1, None, ALU.bitwise_and).then_inc(s_dl, 1)
                dve.wait_ge(s_dl, 1)
                nc.vector.tensor_copy(rel_of_p[:, :], rel_of_p_i[:, :])
                dve.wait_ge(s_ids, 96)
                nc.vector.tensor_reduce(lo, dst_i, AX, ALU.min).then_inc(s_dl, 1)
                nc.vector.tensor_copy(work1, dst_i).then_inc(s_dl, 1)
                dve.wait_ge(s_dl, 3)
                nc.vector.scalar_tensor_tensor(out=xt[:, 0, :], in0=work1[:, etiles - 1, :], scalar=FAR,
                                               in1=work1[:, etiles - 1, :], op0=ALU.is_lt, op1=ALU.mult).then_inc(s_dl, 1)
                nc.vector.tensor_reduce(hi[:, 0:etiles - 1], work1[:, 0:etiles - 1, :], AX, ALU.max).then_inc(s_dl, 1)
                dve.wait_ge(s_dl, 5)
                nc.vector.tensor_reduce(hi[:, etiles - 1:etiles], xt[:, 0, :], AX, ALU.max).then_inc(s_dl, 1)
                nc.vector.tensor_scalar(lo, lo, float(n_nodes), None, ALU.min).then_inc(s_lo, 1)
                dve.wait_ge(s_dl, 6)
                dve.wait_ge(s_lo, 1)
                nc.vector.tensor_tensor(work1, work1, lo.unsqueeze(2).to_broadcast([P, etiles, P]),
                                        ALU.subtract).then_inc(s_relf, 1)
                nc.vector.tensor_tensor(hi, hi, lo, ALU.subtract).then_inc(s_dl, 1)
                dve.wait_ge(s_dl, 7)
                nc.vector.tensor_reduce(wide, hi, AX, ALU.max).then_inc(s_lo, 1)
                for k, (q, m) in enumerate(quads):
                    dve.wait_ge(s_tr, 2 * k + 2)
                    nc.vector.tensor_copy(rel_t[:, q * P:(q + m) * P].rearrange("p (t e) -> p t e", t=m),
                                          tps[1][:, 0:m, :]).then_inc(s_trc, 1)
                for k, (q, m) in enumerate(quads):
                    dve.wait_ge(s_rowp, k + 1)
                    nc.vector.tensor_copy(base[0:1, q * P:(q + m) * P].rearrange("p (t e) -> p t e", t=m),
                                          tps[k % 2][0:1, 0:m, :]).then_inc(s_trc, 1)
                dve.wait_ge(s_trc, 3 * len(quads))
                dve.wait_ge(s_rowp, len(quads) + 1)
                nc.vector.tensor_reduce(std[0:1, 0, 0:1], tps[0][0:1, 0, :], AX, ALU.max).then_inc(s_dl, 1)
                dve.wait_ge(s_dl, 8)
                nc.vector.tensor_copy(span[0:1, :], std[0:1, 0, 0:1]).then_inc(s_dl, 1)
                nc.vector.tensor_copy(base0[0:1, :], base[0:1, :]).then_inc(s_dl, 1)
                dve.wait_ge(s_dl, 10)
                dve.wait_ge(s_w, 16 * (4 + CPG))

            @block.tensor
            def _(pe):
                pe.wait_ge(s_const, 4)
                pe.wait_ge(s_srcf, 1)
                pe.wait_ge(s_relf, 1)
                for k, (q, m) in enumerate(quads):
                    if k:
                        pe.wait_ge(s_trc, 2 * k)
                    for f, (t, w) in enumerate(((tps[0], work0), (tps[1], work1))):
                        for j in range(m):
                            last = nc.tensor.transpose(t[:, j, :], w[:, q + j, :], ident[:, :])
                        last.then_inc(s_tr, 1)
                done = 2 * len(quads)
                pe.wait_ge(s_lo, 2)
                for k, (q, m) in enumerate(quads):
                    pe.wait_ge(s_trc, done + max(k - 1, 0))
                    for j in range(m):
                        last = nc.tensor.matmul(tps[k % 2][0:1, j, :], lo[:, q + j:q + j + 1], ident[:, :],
                                                start=True, stop=True)
                    last.then_inc(s_rowp, 1)
                pe.wait_ge(s_trc, done + len(quads))
                nc.tensor.matmul(tps[0][0:1, 0, :], wide, ident[:, :], start=True, stop=True).then_inc(s_rowp, 1)

        nc.all_engine_barrier()
        span_v = nc.values_load(span[0:1, 0:1], min_val=0, max_val=n_nodes - 1,
                                skip_runtime_bounds_check_because="a difference of two node numbers")

        idx_ready = sem("idx_ready")
        turn = sem("turn")
        gathered = [sem(f"gathered{s}") for s in range(SLOTS)]
        relations_in = [sem(f"relations_in{h}") for h in range(2)]
        relations_tail = sem("relations_tail")
        eoh_ready = sem("eoh_ready")
        wc_ready = sem("wc_ready")
        onehot = sem("onehot")
        a_ready = sem("a_ready")
        z_done = sem("z_done")
        z_copied = sem("z_copied")
        y_done = sem("y_done")
        rmw = sem("rmw")
        group_added = sem("group_added")
        staged = sem("staged")
        turned = sem("turned")
        xt_ready = sem("xt_ready")
        self_done = sem("self_done")
        self_added = sem("self_added")
        moved = sem("moved")
        sweep_sems = range(idx_ready.num, moved.num + 1)

        def gather_groups(pool, table):
            with pool.Fori(0, bodies) as i:
                for u in range(UNROLL):
                    s = u % SLOTS
                    pool.wait_ge(idx_ready, i * UNROLL + u + 1)
                    pool.sem_inc(turn, 1)
                    for c in range(CPG):
                        pool.indirect_dma_start(
                            out=rows[:, s, c, :], out_offset=None, in_=table,
                            in_offset=bass.IndirectOffsetOnAxis(ap=idx[:, s, c:c + 1], axis=0)).then_inc(gathered[s], 16)
            for s in range(SLOTS):
                pool.wait_ge(gathered[s], groups // SLOTS * 16 * CPG)
            pool.dma_reset(range(gathered[0].num, gathered[-1].num + 1))

        def stage_first_indices():
            for s in range(SLOTS):
                nc.scalar.copy(idx[:, s, :], src_t[:, s * CPG:(s + 1) * CPG]).then_inc(idx_ready, 1)

        def stage_indices(i, u):
            nc.scalar.copy(idx[:, u % SLOTS, :],
                           src_t[:, bass.ds((i * UNROLL + u + SLOTS) * CPG, CPG)]).then_inc(idx_ready, 1)

        def rows_in(pe, i, u):
            pe.wait_ge(gathered[u % SLOTS], (i * (UNROLL // SLOTS) + u // SLOTS + 1) * 16 * CPG)

        def make_onehot(i, u):
            r = rel_t[:, bass.ds((i * UNROLL + u) * CPG, CPG)]
            return nc.vector.tensor_tensor(oh1[:, u % 2], r.unsqueeze(2).to_broadcast([P, CPG, WIN]),
                                           lane[:, :].unsqueeze(1).to_broadcast([P, CPG, WIN]), ALU.is_equal)

        def add_group(dve, i, u, ready, sums, kinds):
            _, starts = nc.values_load_multi_w_load_instructions(
                base[0:1, bass.ds((i * UNROLL + u) * CPG, CPG)], engines=DVE_ONLY, min_val=0, max_val=n_nodes,
                skip_runtime_bounds_check_because="clamped to the number of nodes, and acc is padded")
            dve.wait_ge(ready, i * UNROLL + u + 1 + 2)
            dve.wait_ge(group_added, i * UNROLL + u + 2)
            for c in range(CPG):
                target = acc[:, 0:kinds, bass.ds(starts[c], WIN)]
                if c:
                    dve.wait_ge(rmw, i * (UNROLL * (CPG - 1)) + u * (CPG - 1) + c)
                add = nc.vector.tensor_tensor(target, target, sums[:, :, c, :], ALU.add)
                add.then_inc(rmw if c < CPG - 1 else group_added, 1)

        def next_sweep(dve):
            nc.vector.tensor_scalar(lane[:, :], lane[:, :], float(WIN), None, ALU.add).then_inc(moved, 1)
            nc.vector.memset(gate[:, :], 0.0).then_inc(moved, 1)
            nc.vector.tensor_scalar(base[0:1, :], base[0:1, :], float(WIN), float(n_nodes), ALU.add,
                                    ALU.min).then_inc(moved, 1)
            dve.wait_ge(moved, 3)

        with nc.Fori(0, span_v + 1, WIN):
            with nc.Block() as block:
                @block.sync
                def _(sp):
                    def relations(i, h, count):
                        for q in range(count):
                            g0 = (i * UNROLL + h * HALF + q) * group_edges
                            one = etype[g0:g0 + group_edges] if isinstance(g0, int) else etype[bass.ds(g0, group_edges)]
                            sp.dma_start(erep[:, h, q, :],
                                         one.rearrange("(c e) -> c e", c=CPG).unsqueeze(1).to_broadcast([CPG, n_rels, P])
                                         ).then_inc(relations_in[h], 16)

                    for h in range(2):
                        relations(0, h, HALF)
                    with sp.Fori(1, bodies - 1) as i:
                        for h in range(2):
                            sp.wait_ge(eoh_ready, i * 2 + h - 1)
                            relations(i, h, HALF)
                    sp.wait_ge(eoh_ready, (bodies - 1) * 2 - 1)
                    relations(bodies - 1, 0, HALF)
                    sp.wait_ge(eoh_ready, (bodies - 1) * 2)
                    e0 = full_chunks * P
                    part = last_group_chunks * n_rels
                    sp.dma_start(erep[part:part + n_rels, 1, HALF - 1, 0:rest_edges],
                                 etype[e0:n_edges].rearrange("(c e) -> c e", c=1).to_broadcast([n_rels, rest_edges])
                                 ).then_inc(relations_tail, 16)
                    sp.wait_ge(relations_tail, 16)
                    relations(bodies - 1, 1, HALF - 1)
                    g0 = last_group * group_edges
                    sp.dma_start(erep[0:part, 1, HALF - 1, :],
                                 etype[g0:e0].rearrange("(c e) -> c e", e=P).unsqueeze(1).to_broadcast([last_group_chunks, n_rels, P])
                                 ).then_inc(relations_in[1], 16)

                @block.gpsimd
                def _(pool):
                    gather_groups(pool, x_in)

                @block.scalar
                def _(act):
                    act.sem_inc(z_copied, 2)
                    stage_first_indices()
                    with act.Fori(0, bodies) as i:
                        for u in range(UNROLL):
                            g = i * UNROLL + u
                            act.wait_ge(y_done, g + 1)
                            act.wait_ge(z_done, g + 1 + 2)
                            nc.scalar.copy(zsb[:, u % 2], zps[u % 2][:, :, :, :]).then_inc(z_copied, 1)
                            stage_indices(i, u)

                @block.vector
                def _(dve):
                    dve.sem_inc(a_ready, UNROLL)
                    dve.sem_inc(group_added, 2)
                    with dve.Fori(0, bodies) as i:
                        for u in range(UNROLL):
                            g = i * UNROLL + u
                            h = u // HALF
                            if u % HALF == 0:
                                dve.wait_ge(wc_ready, i * 2 + h + 1)
                                dve.wait_ge(relations_in[h], (i + 1) * 16 * HALF)
                                nc.vector.tensor_scalar(eoh[:, h], erep[:, h], rel_of_p[:, 0:1], None,
                                                        ALU.is_equal).then_inc(eoh_ready, 1)
                            make_onehot(i, u).then_inc(onehot, 1)
                            dve.wait_ge(z_done, g + 1)
                            dve.wait_ge(wc_ready, i * 2 + h + 1 + 2)
                            dve.wait_ge(onehot, g + 1)
                            nc.vector.tensor_tensor(
                                a[:, u % 2], oh1[:, u % 2].unsqueeze(2).to_broadcast([P, CPG, n_bases, WIN]),
                                wcp[h][:, u % HALF, :].rearrange("p (c b) -> p c b", c=CPG).unsqueeze(3)
                                .to_broadcast([P, CPG, n_bases, WIN]), ALU.mult).then_inc(a_ready, 1)
                            if u >= 2:
                                add_group(dve, i, u - 2, y_done, yps[u % 2][:, 0:1], 1)
                        for u in (UNROLL - 2, UNROLL - 1):
                            add_group(dve, i, u, y_done, yps[u % 2][:, 0:1], 1)
                    dve.wait_ge(group_added, groups + 2)
                    next_sweep(dve)

                @block.tensor
                def _(pe):
                    pe.sem_inc(wc_ready, 2)
                    pe.sem_inc(z_done, 2)
                    pe.sem_inc(y_done, 2)

                    def project(i, u):
                        g = i * UNROLL + u
                        pe.wait_ge(group_added, g + 1)
                        pe.wait_ge(z_copied, g + 1 + 2)
                        for b in range(n_bases):
                            last = nc.tensor.matmul(yps[u % 2][:, 0], wb[:, b, :], zsb[:, u % 2, :, b, :],
                                                    start=(b == 0), stop=(b == n_bases - 1))
                        last.then_inc(y_done, 1)

                    with pe.Fori(0, bodies) as i:
                        for u in range(UNROLL):
                            g = i * UNROLL + u
                            h = u // HALF
                            if u % HALF == 0:
                                pe.wait_ge(a_ready, i * UNROLL + (h + 1) * HALF)
                                pe.wait_ge(eoh_ready, i * 2 + h + 1)
                                for q in range(HALF):
                                    last = nc.tensor.matmul(wcp[h][:, q, :], eoh[:, h, q, :],
                                                            wc_blk[:, :, :].rearrange("p c b -> p (c b)"),
                                                            start=True, stop=True)
                                last.then_inc(wc_ready, 1)
                            pe.wait_ge(z_copied, g + 1)
                            pe.wait_ge(a_ready, g + 1 + UNROLL)
                            rows_in(pe, i, u)
                            for c in range(CPG):
                                last = nc.tensor.matmul(zps[u % 2][:, c], rows[:, u % SLOTS, c, :], a[:, u % 2, c],
                                                        start=True, stop=True)
                            last.then_inc(z_done, 1)
                            if u:
                                project(i, u - 1)
                        project(i, UNROLL - 1)

            nc.all_engine_barrier(sems_to_clear=sweep_sems)

        step_v = sem("step_v")
        step_p = sem("step_p")
        step_a = sem("step_a")
        s_stage = sem("s_stage")
        s_product = sem("s_product")
        s_base = sem("s_base")
        s_deg = sem("s_deg")
        s_rdeg = sem("s_rdeg")
        s_added = sem("s_added")
        s_bn = sem("s_bn")
        s_stats = sem("s_stats")
        s_std = sem("s_std")
        s_rstd = sem("s_rstd")
        s_factors = sem("s_factors")
        s_norm = sem("s_norm")
        s_zero = sem("s_zero")
        s_rows = sem("s_rows")
        norm_sems = range(s_stage.num, s_rows.num + 1)
        out_stored = sem("out_stored")

        def tile_stats(dve, i, h):
            k = i * 2 + h
            dve.wait_ge(s_added, k + 1 + 2)
            dve.sem_inc(step_v, 1)
            for j in range(TPH):
                last = nc.vector.bn_stats(stats[:, h, j, :], nodes[:, bass.ds(k * TPH + j, 1), :])
            last.then_inc(s_bn, 1)
            dve.wait_ge(s_bn, k + 1)
            dve.sem_inc(step_v, 1)
            for j in range(TPH):
                last = nc.vector.bn_aggr(mv[:, h, j, :], stats[:, h, j, :])
            last.then_inc(s_stats, 1)

        def tile_factors(dve, i, h):
            k = i * 2 + h
            dve.wait_ge(s_norm, k + 1)
            dve.wait_ge(s_std, k + 1)
            nc.vector.reciprocal(rstd[:, h, :], std[:, h, :]).then_inc(s_rstd, 1)
            dve.wait_ge(s_rstd, k + 1)
            nc.vector.scalar_tensor_tensor(out=shift[:, h, :], in0=mv[:, h, :, 0], scalar=-1.0, in1=rstd[:, h, :],
                                           op0=ALU.mult, op1=ALU.mult).then_inc(s_factors, 1)

        def roots(act, i, h):
            act.wait_ge(s_stats, i * 2 + h + 1)
            nc.scalar.activation(std[:, h, :], mv[:, h, :, 1], ACT.Sqrt, bias=epst[:, 0:1],
                                 scale=1.0).then_inc(s_std, 1)

        def normalise(act, i, h):
            k = i * 2 + h
            act.wait_ge(s_factors, k + 1)
            act.sem_inc(step_a, 1)
            for j in range(TPH):
                t = nodes[:, bass.ds(k * TPH + j, 1), :]
                last = nc.scalar.activation(t, t, ACT.Identity, bias=shift[:, h, j:j + 1], scale=rstd[:, h, j:j + 1])
            last.then_inc(s_norm, 1)

        with nc.Block() as block:
            @block.scalar
            def _(act):
                act.sem_inc(s_norm, 2)
                with act.Fori(0, nbodies) as i:
                    for h in range(2):
                        k = i * 2 + h
                        act.wait_ge(s_product, k + 1)
                        nc.scalar.copy(stage[:, h], acc[:, 0, bass.ds(k * (TPH * P), TPH * P)]).then_inc(s_stage, 1)
                    for h in range(2):
                        roots(act, i, h)
                    for h in range(2):
                        normalise(act, i, h)

            @block.tensor
            def _(pe):
                pe.sem_inc(s_product, 2)
                with pe.Fori(0, nbodies) as i:
                    for h in range(2):
                        k = i * 2 + h
                        pe.wait_ge(s_added, k + 1)
                        pe.wait_ge(s_stage, k + 1)
                        for j in range(TPH):
                            last = nc.tensor.transpose(tps[h][:, j, :], stage[:, h, j, :], ident[:, :])
                        last.then_inc(s_product, 1)

            @block.vector
            def _(dve):
                dve.sem_inc(s_added, 2)
                nc.vector.tensor_copy(base[0:1, :], base0[0:1, :]).then_inc(s_base, 1)
                nc.vector.tensor_copy(lane[:, :], lane_i[:, :])
                nc.vector.memset(gate[:, :], 1.0)
                dve.wait_ge(s_x, 32)
                with dve.Fori(0, nbodies) as i:
                    for h in range(2):
                        k = i * 2 + h
                        four = nodes[:, bass.ds(k * TPH, TPH), :]
                        dve.wait_ge(s_product, k + 1 + 2)
                        nc.vector.tensor_tensor(four, four, tps[h][:, :, :], ALU.add).then_inc(s_added, 1)
                        tile_stats(dve, i, h)
                    for h in range(2):
                        tile_factors(dve, i, h)

            @block.gpsimd
            def _(pool):
                pool.wait_ge(s_base, 1)
                with pool.Fori(0, nbodies) as i:
                    for h in range(2):
                        k = i * 2 + h
                        pool.wait_ge(s_stage, k + 1)
                        pool.sem_inc(step_p, 1)
                        nc.gpsimd.tensor_copy(acc[:, :, bass.ds(k * (TPH * P), TPH * P)],
                                              zero[:, 0:1].unsqueeze(2).to_broadcast([P, 2, TPH * P]))

            @block.sync
            def _(sp):
                with sp.Fori(0, nbodies) as i:
                    for h in range(2):
                        k = i * 2 + h
                        sp.wait_ge(s_norm, k + 1 + 2)
                        sp.dma_start(x1_rows[bass.ds(k * (TPH * P), TPH * P), :].rearrange("(t p) f -> p t f", p=P),
                                     nodes[:, bass.ds(k * TPH, TPH), :]).then_inc(s_rows, 16)
                sp.wait_ge(s_rows, tiles_p // TPH * 16)

        nc.all_engine_barrier(sems_to_clear=norm_sems)

        with nc.Fori(0, span_v + 1, WIN):
            with nc.Block() as block:
                @block.gpsimd
                def _(pool):
                    gather_groups(pool, x1_rows)

                @block.scalar
                def _(act):
                    act.sem_inc(xt_ready, 1)
                    stage_first_indices()
                    with act.Fori(0, bodies) as i:
                        for u in range(UNROLL):
                            if u == 0:
                                act.wait_ge(turned, i + 1)
                                nc.scalar.copy(stage[:, 0], nodes[:, bass.ds(i * TPH, TPH), :]).then_inc(staged, 1)
                            if u == 3:
                                act.wait_ge(self_done, i + 1)
                                act.wait_ge(turned, i + 1 + 1)
                                nc.scalar.copy(xt[:, :, :], tps[0][:, :, :]).then_inc(xt_ready, 1)
                            act.wait_ge(z_done, i * UNROLL + u + 1 + 2)
                            stage_indices(i, u)

                @block.vector
                def _(dve):
                    dve.sem_inc(group_added, 2)
                    dve.sem_inc(self_added, 1)
                    with dve.Fori(0, bodies) as i:
                        for u in range(UNROLL):
                            g = i * UNROLL + u
                            dve.wait_ge(z_done, g + 1)
                            make_onehot(i, u).then_inc(a_ready, 1)
                            if u == 6:
                                four = nodes[:, bass.ds(i * TPH, TPH), :]
                                dve.wait_ge(self_done, i + 1 + 1)
                                nc.vector.scalar_tensor_tensor(out=four, in0=tps[1][:, :, :], scalar=gate[:, 0:1],
                                                               in1=four, op0=ALU.mult, op1=ALU.add
                                                               ).then_inc(self_added, 1)
                            if u >= 2:
                                add_group(dve, i, u - 2, z_done, yps[u % 2], 2)
                        for u in (UNROLL - 2, UNROLL - 1):
                            add_group(dve, i, u, z_done, yps[u % 2], 2)
                    dve.wait_ge(group_added, groups + 2)
                    next_sweep(dve)

                @block.tensor
                def _(pe):
                    pe.sem_inc(z_done, 2)
                    pe.sem_inc(turned, 1)
                    pe.sem_inc(self_done, 1)
                    with pe.Fori(0, bodies) as i:
                        for u in range(UNROLL):
                            g = i * UNROLL + u
                            pe.wait_ge(group_added, g + 1)
                            pe.wait_ge(a_ready, g + 1)
                            nc.tensor.matmul(yps[u % 2][:, 1], onesm[:, :], oh1[:, u % 2], start=True, stop=True)
                            rows_in(pe, i, u)
                            for c in range(CPG):
                                last = nc.tensor.matmul(yps[u % 2][:, 0, c], rows[:, u % SLOTS, c, :], oh1[:, u % 2, c],
                                                        start=True, stop=True)
                            last.then_inc(z_done, 1)
                            if u == 1:
                                pe.wait_ge(xt_ready, i + 1)
                                pe.wait_ge(staged, i + 1)
                                for j in range(TPH):
                                    last = nc.tensor.transpose(tps[0][:, j, :], stage[:, 0, j, :], ident[:, :])
                                last.then_inc(turned, 1)
                            if u == 4:
                                pe.wait_ge(self_added, i + 1)
                                pe.wait_ge(xt_ready, i + 1 + 1)
                                for j in range(TPH):
                                    nc.tensor.matmul(tps[1][:, j, :], xt[:, j, :], ws[:, :], start=True, stop=False)
                                    last = nc.tensor.matmul(tps[1][:, j, :], onesm[0:1, :], bself[0:1, :],
                                                            start=False, stop=True)
                                last.then_inc(self_done, 1)

            nc.all_engine_barrier(sems_to_clear=sweep_sems)

        with nc.Block() as block:
            @block.scalar
            def _(act):
                act.sem_inc(s_norm, 2)
                with act.Fori(0, nbodies) as i:
                    for h in range(2):
                        k = i * 2 + h
                        tiles = bass.ds(k * (TPH * P), TPH * P)
                        act.wait_ge(s_product, k + 1)
                        nc.scalar.copy(deg_st[0:1, h], acc[0:1, 1, tiles])
                        nc.scalar.copy(stage[:, h], acc[:, 0, tiles]).then_inc(s_stage, 1)
                    for h in range(2):
                        roots(act, i, h)
                    for h in range(2):
                        normalise(act, i, h)

            @block.tensor
            def _(pe):
                pe.sem_inc(s_product, 2)
                with pe.Fori(0, nbodies) as i:
                    for h in range(2):
                        k = i * 2 + h
                        pe.wait_ge(s_added, k + 1)
                        pe.wait_ge(s_stage, k + 1)
                        for j in range(TPH):
                            nc.tensor.matmul(yps[h][:, 0, 0, j:j + 1], deg_st[0:1, h, j, :], onesm[0:1, 0:1],
                                             start=True, stop=True)
                        for j in range(TPH):
                            last = nc.tensor.matmul(tps[h][:, j, :], stage[:, h, j, :], wn[:, :], start=True, stop=True)
                        last.then_inc(s_product, 1)

            @block.vector
            def _(dve):
                dve.sem_inc(s_added, 2)
                with dve.Fori(0, nbodies) as i:
                    for h in range(2):
                        k = i * 2 + h
                        dve.wait_ge(s_product, k + 1 + 2)
                        nc.vector.tensor_scalar(rdeg[:, h, :], yps[h][:, 0, 0, 0:TPH], 1.0, None, ALU.max).then_inc(s_deg, 1)
                        dve.wait_ge(s_deg, k + 1)
                        nc.vector.reciprocal(rdeg[:, h, :], rdeg[:, h, :]).then_inc(s_rdeg, 1)
                        dve.wait_ge(s_rdeg, k + 1)
                        for j in range(TPH):
                            t = nodes[:, bass.ds(k * TPH + j, 1), :].rearrange("p o f -> p (o f)")
                            last = nc.vector.scalar_tensor_tensor(out=t, in0=tps[h][:, j, :], scalar=rdeg[:, h, j:j + 1],
                                                                  in1=t, op0=ALU.mult, op1=ALU.add)
                        last.then_inc(s_added, 1)
                        tile_stats(dve, i, h)
                    for h in range(2):
                        tile_factors(dve, i, h)

            @block.sync
            def _(sp):
                whole = full_ntiles // TPH
                assert whole % 2 == 0 and full_ntiles % TPH == 1
                with sp.Fori(0, whole // 2) as i:
                    for h in range(2):
                        k = i * 2 + h
                        sp.wait_ge(s_norm, k + 1 + 2)
                        sp.dma_start(out[bass.ds(k * (TPH * P), TPH * P), :].rearrange("(t p) f -> p t f", p=P),
                                     nodes[:, bass.ds(k * TPH, TPH), :]).then_inc(out_stored, 16)
                sp.wait_ge(s_norm, whole + 1 + 2)
                sp.dma_start(out[whole * TPH * P:full_ntiles * P, :], nodes[:, full_ntiles - 1, :]).then_inc(out_stored, 16)
                sp.dma_start(out[full_ntiles * P:n_nodes, :], nodes[0:rest_nodes, full_ntiles, :]).then_inc(out_stored, 16)
                sp.wait_ge(out_stored, (whole + 2) * 16)


_INS = ["x", "src", "dst", "edge_type_16", "L0_gnn_weight", "L0_gnn_w_comp", "L0_gnn_h_bias", "L1_gnn_W_neigh",
        "L1_gnn_W_self", "L1_gnn_b_self"]


def kernel(**inputs):
    import numpy as _np
    import concourse.bacc as _bacc
    from concourse import mybir as _mybir
    from concourse.bass_utils import run_bass_kernel_spmd as _run

    nc = _bacc.Bacc("TRN2", target_bir_lowering=False, num_devices=1)
    arrays, args = {}, []
    for name in _INS:
        a = _np.ascontiguousarray(inputs[name])
        arrays[f"in_{name}_dram"] = a
        args.append(nc.dram_tensor(f"in_{name}_dram", a.shape, _mybir.dt.from_np(a.dtype), kind="ExternalInput").ap())
    n_nodes, d = inputs["x"].shape
    step = P * UNROLL
    x1_rows = nc.dram_tensor("x1_rows", (-(-n_nodes // step) * step, d), F32, kind="Internal").ap()
    out = nc.dram_tensor("out_dram", (n_nodes, d), F32, kind="ExternalOutput").ap()
    gnn_kernel(nc, *args, x1_rows, out)
    r = _run(nc, [arrays], core_ids=[0])
    return r.results[0]["out_dram"]
```

```python
import concourse.bass as bass
from concourse import mybir
from contextlib import ExitStack

F32 = mybir.dt.float32
I32 = mybir.dt.int32
ALU = mybir.AluOpType
ACT = mybir.ActivationFunctionType
AX = mybir.AxisListType.X
DVE_ONLY = [mybir.EngineType.DVE]

P = 128
WIN = 16
CPG = 8
UNROLL = 8
SLOTS = 4
TPH = 4
QUAD = TPH * P
LAG = 3
FAR = 65536.0
EPS = 1e-5


def gnn_kernel(nc, x_in, src, dst, etype, weight, w_comp, h_bias, w_neigh, w_self, b_self, x1_rows, out):
    n_nodes, d = x_in.shape
    (n_edges,) = src.shape
    n_bases = weight.shape[0]
    n_rels = w_comp.shape[0]
    assert d == P and n_rels * CPG == P and weight.shape[1] == d and weight.shape[2] == d

    group_edges = CPG * P
    full_chunks = n_edges // P
    rest_edges = n_edges - full_chunks * P
    etiles = -(-n_edges // (P * P))
    chunks = etiles * P
    groups = chunks // CPG
    bodies = groups // UNROLL
    last_tile_chunks = full_chunks - (etiles - 1) * P
    assert 0 < last_tile_chunks < P and rest_edges > 0 and groups % UNROLL == 0
    last_group = groups - 1
    last_group_chunks = full_chunks - last_group * CPG
    assert 0 < last_group_chunks < CPG

    ntiles = -(-n_nodes // P)
    full_ntiles = n_nodes // P
    rest_nodes = n_nodes - full_ntiles * P
    tiles_p = -(-ntiles // UNROLL) * UNROLL
    nodes_p = tiles_p * P
    nbodies = tiles_p // UNROLL
    assert nodes_p >= n_nodes + WIN and rest_nodes > 0 and tiles_p == TPH * bodies
    GW = CPG * WIN
    HALF = UNROLL // 2

    ctx = ExitStack()
    with ctx:
        def sb(name, shape, dt=F32):
            return ctx.enter_context(nc.sbuf_tensor(name, shape, dt))

        def pb(name, shape):
            return ctx.enter_context(nc.psum_tensor(name, shape, F32))

        def sem(name):
            return ctx.enter_context(nc.semaphore(name))

        acc = sb("acc", [P, 2, nodes_p])
        nodes = sb("nodes", [P, tiles_p, d])
        rows = sb("rows", [P, SLOTS, CPG, d])
        idx = sb("idx", [P, SLOTS, CPG], I32)
        src_t = sb("src_t", [P, chunks + SLOTS * CPG], I32)
        rel_t = sb("rel_t", [P, chunks])
        base = sb("base", [1, chunks], I32)
        span = sb("span", [1, 2], I32)
        ident = sb("ident", [P, P])
        onesm = sb("onesm", [P, P])
        lane_i = sb("lane_i", [P, WIN], I32)
        lane = sb("lane", [P, WIN])
        part_i = sb("part_i", [P, 1], I32)
        rel_of_p_i = sb("rel_of_p_i", [P, 1], I32)
        rel_of_p = sb("rel_of_p", [P, 1])
        wc_blk = sb("wc_blk", [P, CPG, n_bases])
        gate = sb("gate", [P, 1])
        bias_col = sb("bias_col", [P, 1])
        bself = sb("bself", [1, d])
        wn = sb("wn", [P, d])
        ws = sb("ws", [P, d])
        stage = sb("stage", [P, 2, TPH, P])
        xt = sb("xt", [P, TPH, P])
        deg_st = sb("deg_st", [1, 2, TPH, P])
        stats = sb("stats", [P, 2, TPH, 6])
        mv = sb("mv", [P, 2, TPH, 2])
        std = sb("std", [P, 2, TPH])
        rstd = sb("rstd", [P, 2, TPH])
        shift = sb("shift", [P, 2, TPH])
        rdeg = sb("rdeg", [P, 2, TPH])
        epst = sb("epst", [P, 1])
        due_i = sb("due_i", [P, etiles], I32)
        due = sb("due", [P, etiles])
        late = sb("late", [P, 2])
        flags = sb("flags", [1, 4])
        zero = sb("zero", [P, 1])
        oh1 = sb("oh1", [P, 2, CPG, WIN])

        taken = [0]

        def first_layer(words):
            taken[0] += words
            assert taken[0] <= nodes_p
            return acc[:, 1, taken[0] - words:taken[0]]

        a = first_layer(2 * CPG * n_bases * WIN).rearrange("p (u c b n) -> p u c b n", u=2, c=CPG, b=n_bases)
        zsb = first_layer(2 * CPG * n_bases * WIN).rearrange("p (u c b n) -> p u c b n", u=2, c=CPG, b=n_bases)
        eoh = first_layer(2 * HALF * P).rearrange("p (h q e) -> p h q e", h=2, q=HALF)
        erep = first_layer(2 * HALF * P).rearrange("p (h q e) -> p h q e", h=2, q=HALF).bitcast(I32)
        wb = first_layer(n_bases * d).rearrange("p (b o) -> p b o", b=n_bases)
        work0 = first_layer(chunks).rearrange("p (t e) -> p t e", t=etiles)
        work1 = first_layer(chunks).rearrange("p (t e) -> p t e", t=etiles)
        work2 = acc[:, 1, 0:chunks].rearrange("p (t e) -> p t e", t=etiles)
        base0 = first_layer(chunks).bitcast(I32)
        src_i = rows[:, 0:2].rearrange("p s c e -> p (s c e)")[:, 0:chunks].rearrange("p (t e) -> p t e", t=etiles).bitcast(I32)
        dst_i = rows[:, 2:4].rearrange("p s c e -> p (s c e)")[:, 0:chunks].rearrange("p (t e) -> p t e", t=etiles).bitcast(I32)
        lo = stats[:, 0, :, :].rearrange("p a b -> p (a b)")[:, 0:etiles]
        hi = stats[:, 1, :, :].rearrange("p a b -> p (a b)")[:, 0:etiles]
        wide = mv[:, 0, 0, 0:1]

        zps = [pb(f"zps{i}", [P, CPG, n_bases, WIN]) for i in range(2)]
        yps = [pb(f"yps{i}", [P, 2, 2, CPG, WIN])[:, 0] for i in range(2)]
        tps = [pb(f"tps{i}", [P, TPH, P]) for i in range(2)]
        wcp = tps[0][:, :, :].rearrange("p t e -> p (t e)").rearrange("p (h q k) -> p h q k", h=2, q=HALF)
        zbanks = [z[:, :, :, :].rearrange("p c b n -> p (c b n)").rearrange("p (k t e) -> p k t e", k=2, t=TPH)
                  for z in zps]

        s_pad = sem("s_pad")
        s_ids = sem("s_ids")
        s_w = sem("s_w")
        s_x = sem("s_x")
        s_const = sem("s_const")
        s_blk0 = sem("s_blk0")
        s_bias = sem("s_bias")
        s_pl = sem("s_pl")
        s_dl = sem("s_dl")
        s_al = sem("s_al")
        s_srcf = sem("s_srcf")
        s_relf = sem("s_relf")
        s_lo = sem("s_lo")
        s_tr = sem("s_tr")
        s_trc = sem("s_trc")
        s_rowp = sem("s_rowp")
        quads = [(q, min(TPH, etiles - q)) for q in range(0, etiles, TPH)]

        with nc.Block() as block:
            @block.sync
            def _(sp):
                sp.wait_ge(s_pad, 3)
                for dram, tile in ((dst, dst_i), (src, src_i)):
                    sp.dma_start(tile[:, 0:etiles - 1, :],
                                 dram[0:(etiles - 1) * P * P].rearrange("(t p e) -> p t e", p=P, e=P)).then_inc(s_ids, 16)
                    sp.dma_start(tile[0:last_tile_chunks, etiles - 1, :],
                                 dram[(etiles - 1) * P * P:full_chunks * P].rearrange("(p e) -> p e", e=P)).then_inc(s_ids, 16)
                    sp.dma_start(tile[last_tile_chunks:last_tile_chunks + 1, etiles - 1, 0:rest_edges],
                                 dram[full_chunks * P:n_edges].rearrange("(p e) -> p e", p=1)).then_inc(s_ids, 16)
                sp.dma_start(bias_col[:, :], h_bias.rearrange("(p o) -> p o", o=1)).then_inc(s_bias, 16)
                sp.dma_start(wb, weight.rearrange("b i o -> i b o")).then_inc(s_w, 16)
                sp.dma_start(wn[:, :], w_neigh).then_inc(s_w, 16)
                sp.dma_start(ws[:, :], w_self).then_inc(s_w, 16)
                sp.dma_start(bself[0:1, :], b_self.rearrange("(p o) -> p o", p=1)).then_inc(s_w, 16)
                sp.wait_ge(s_blk0, 1)
                for c in range(CPG):
                    sp.dma_start(wc_blk[c * n_rels:(c + 1) * n_rels, c, :], w_comp).then_inc(s_w, 16)
                sp.dma_start(nodes[0:rest_nodes, full_ntiles, :], x_in[full_ntiles * P:n_nodes, :]).then_inc(s_x, 16)
                sp.dma_start(nodes[:, 0:full_ntiles, :],
                             x_in[0:full_ntiles * P, :].rearrange("(t p) f -> p t f", p=P)).then_inc(s_x, 16)

            @block.gpsimd
            def _(pool):
                nc.gpsimd.iota(lane_i[:, :], pattern=[[1, WIN]], base=0, channel_multiplier=0).then_inc(s_const, 1)
                nc.gpsimd.iota(part_i[:, :], pattern=[[0, 1]], base=0, channel_multiplier=1).then_inc(s_const, 1)
                nc.gpsimd.iota(due_i[:, :], pattern=[[2 * QUAD, etiles]], base=(1 - LAG) * QUAD,
                               channel_multiplier=0).then_inc(s_const, 1)
                nc.gpsimd.memset(ident[:, :], 0.0).then_inc(s_pl, 1)
                pool.wait_ge(s_pl, 1)
                nc.gpsimd.affine_select(out=ident[:, :], in_=ident[:, :], compare_op=ALU.not_equal, fill=1.0, base=0,
                                        pattern=[[-1, P]], channel_multiplier=1).then_inc(s_const, 1)
                nc.gpsimd.memset(wc_blk[:, :, :], 0.0).then_inc(s_blk0, 1)
                nc.gpsimd.memset(src_t[:, chunks:chunks + SLOTS * CPG], 0)
                nc.gpsimd.memset(erep, 0).then_inc(s_const, 1)

            @block.scalar
            def _(act):
                act.wait_ge(s_dl, 1)
                act.wait_ge(s_ids, 96)
                nc.scalar.copy(work0, src_i).then_inc(s_srcf, 1)
                for k, (q, m) in enumerate(quads):
                    act.wait_ge(s_tr, 2 * k + 1)
                    nc.scalar.copy(src_t[:, q * P:(q + m) * P], tps[0][:, 0:m, :]).then_inc(s_trc, 1)
                nc.scalar.activation(std[:, 1, 0:1], onesm[:, 0:1], ACT.Sqrt).then_inc(s_al, 1)
                act.wait_ge(s_al, 1)

            @block.vector
            def _(dve):
                nc.vector.memset(dst_i[:, etiles - 1, :], int(FAR)).then_inc(s_pad, 1)
                nc.vector.memset(src_i[:, etiles - 1, :], 0).then_inc(s_pad, 1)
                nc.vector.memset(nodes[:, full_ntiles:tiles_p, :], 0.0).then_inc(s_pad, 1)
                nc.vector.memset(onesm[:, :], 1.0)
                nc.vector.memset(gate[:, :], 1.0)
                nc.vector.memset(epst[:, :], EPS)
                nc.vector.memset(zero[:, :], 0.0)
                dve.wait_ge(s_const, 5)
                nc.vector.tensor_copy(lane[:, :], lane_i[:, :])
                nc.vector.tensor_scalar(rel_of_p_i[:, :], part_i[:, :], n_rels - 1, None, ALU.bitwise_and).then_inc(s_dl, 1)
                nc.vector.tensor_copy(due[:, :], due_i[:, :]).then_inc(s_dl, 1)
                nc.vector.tensor_copy(late[:, 0:1], part_i[:, :]).then_inc(s_dl, 1)
                dve.wait_ge(s_dl, 3)
                nc.vector.tensor_scalar(late[:, 1:2], late[:, 0:1], float(P // 2), float(QUAD), ALU.is_ge,
                                        ALU.mult).then_inc(s_dl, 1)
                dve.wait_ge(s_dl, 4)
                nc.vector.tensor_scalar(due[:, :], due[:, :], late[:, 1:2], None, ALU.add).then_inc(s_dl, 1)
                nc.vector.tensor_copy(rel_of_p[:, :], rel_of_p_i[:, :])
                dve.wait_ge(s_ids, 96)
                nc.vector.tensor_reduce(lo, dst_i, AX, ALU.min).then_inc(s_dl, 1)
                nc.vector.tensor_copy(work1, dst_i).then_inc(s_dl, 1)
                dve.wait_ge(s_dl, 7)
                nc.vector.tensor_scalar(lo, lo, float(n_nodes), None, ALU.min).then_inc(s_lo, 1)
                dve.wait_ge(s_lo, 1)
                nc.vector.tensor_tensor(work2, work1, lo.unsqueeze(2).to_broadcast([P, etiles, P]),
                                        ALU.subtract).then_inc(s_relf, 1)
                nc.vector.scalar_tensor_tensor(out=xt[:, 0, :], in0=work1[:, etiles - 1, :], scalar=FAR,
                                               in1=work1[:, etiles - 1, :], op0=ALU.is_lt, op1=ALU.mult).then_inc(s_dl, 1)
                nc.vector.tensor_reduce(hi[:, 0:etiles - 1], work1[:, 0:etiles - 1, :], AX, ALU.max).then_inc(s_dl, 1)
                dve.wait_ge(s_dl, 9)
                nc.vector.tensor_reduce(hi[:, etiles - 1:etiles], xt[:, 0, :], AX, ALU.max).then_inc(s_dl, 1)
                nc.vector.tensor_tensor(due[:, :], due[:, :], lo, ALU.subtract).then_inc(s_dl, 1)
                dve.wait_ge(s_dl, 11)
                nc.vector.tensor_tensor(hi, hi, lo, ALU.subtract).then_inc(s_dl, 1)
                nc.vector.tensor_reduce(late[:, 0:1], due[:, :], AX, ALU.max).then_inc(s_dl, 1)
                dve.wait_ge(s_dl, 13)
                nc.vector.tensor_reduce(wide, hi, AX, ALU.max).then_inc(s_lo, 1)
                for k, (q, m) in enumerate(quads):
                    dve.wait_ge(s_tr, 2 * k + 2)
                    nc.vector.tensor_copy(rel_t[:, q * P:(q + m) * P].rearrange("p (t e) -> p t e", t=m),
                                          tps[1][:, 0:m, :]).then_inc(s_trc, 1)
                for k, (q, m) in enumerate(quads):
                    dve.wait_ge(s_rowp, k + 1)
                    nc.vector.tensor_copy(base[0:1, q * P:(q + m) * P].rearrange("p (t e) -> p t e", t=m),
                                          tps[k % 2][0:1, 0:m, :]).then_inc(s_trc, 1)
                dve.wait_ge(s_trc, 3 * len(quads))
                dve.wait_ge(s_rowp, len(quads) + 1)
                nc.vector.tensor_reduce(flags[0:1, 0:2], tps[0][0:1, 0:2, :], AX, ALU.max).then_inc(s_dl, 1)
                dve.wait_ge(s_dl, 14)
                nc.vector.tensor_copy(span[0:1, 0:1], flags[0:1, 0:1]).then_inc(s_dl, 1)
                nc.vector.tensor_scalar(flags[0:1, 2:3], flags[0:1, 0:1], float(WIN), None, ALU.is_lt).then_inc(s_dl, 1)
                dve.wait_ge(s_dl, 16)
                nc.vector.scalar_tensor_tensor(out=span[0:1, 1:2], in0=flags[0:1, 1:2], scalar=0.0,
                                               in1=flags[0:1, 2:3], op0=ALU.is_le, op1=ALU.mult).then_inc(s_dl, 1)
                dve.wait_ge(s_dl, 17)
                dve.wait_ge(s_w, 16 * (4 + CPG))
                dve.wait_ge(s_bias, 16)

            @block.tensor
            def _(pe):
                pe.wait_ge(s_const, 5)
                pe.wait_ge(s_srcf, 1)
                pe.wait_ge(s_relf, 1)
                for k, (q, m) in enumerate(quads):
                    if k:
                        pe.wait_ge(s_trc, 2 * k)
                    for f, (t, w) in enumerate(((tps[0], work0), (tps[1], work2))):
                        for j in range(m):
                            last = nc.tensor.transpose(t[:, j, :], w[:, q + j, :], ident[:, :])
                        last.then_inc(s_tr, 1)
                done = 2 * len(quads)
                pe.wait_ge(s_lo, 2)
                for k, (q, m) in enumerate(quads):
                    pe.wait_ge(s_trc, done + max(k - 1, 0))
                    for j in range(m):
                        last = nc.tensor.matmul(tps[k % 2][0:1, j, :], lo[:, q + j:q + j + 1], ident[:, :],
                                                start=True, stop=True)
                    last.then_inc(s_rowp, 1)
                pe.wait_ge(s_trc, done + len(quads))
                nc.tensor.matmul(tps[0][0:1, 0, :], wide, ident[:, :], start=True, stop=True)
                nc.tensor.matmul(tps[0][0:1, 1, :], late[:, 0:1], ident[:, :], start=True, stop=True).then_inc(s_rowp, 1)

        nc.all_engine_barrier()
        span_v = nc.values_load(span[0:1, 0:1], min_val=0, max_val=n_nodes - 1,
                                skip_runtime_bounds_check_because="a difference of two node numbers")
        in_order = nc.values_load(span[0:1, 1:2], min_val=0, max_val=1,
                                  skip_runtime_bounds_check_because="a comparison's result")


        class Sweep:

            def __init__(self, n):
                self.idx_ready = sem(f"idx_ready{n}")
                self.turn = sem(f"turn{n}")
                self.gathered = [sem(f"gathered{n}_{s}") for s in range(SLOTS)]
                self.relations_in = [sem(f"relations_in{n}_{h}") for h in range(2)]
                self.relations_tail = sem(f"relations_tail{n}")
                self.eoh_ready = sem(f"eoh_ready{n}")
                self.wc_ready = sem(f"wc_ready{n}")
                self.onehot = sem(f"onehot{n}")
                self.a_ready = sem(f"a_ready{n}")
                self.z_done = sem(f"z_done{n}")
                self.z_copied = sem(f"z_copied{n}")
                self.y_done = sem(f"y_done{n}")
                self.rmw = sem(f"rmw{n}")
                self.group_added = sem(f"group_added{n}")
                self.staged = sem(f"staged{n}")
                self.turned = sem(f"turned{n}")
                self.xt_ready = sem(f"xt_ready{n}")
                self.self_done = sem(f"self_done{n}")
                self.self_added = sem(f"self_added{n}")
                self.moved = sem(f"moved{n}")
                self.all = range(self.idx_ready.num, self.moved.num + 1)

        class Norm:

            def __init__(self, n, depth):
                self.depth = depth
                self.step_v = sem(f"step_v{n}")
                self.step_a = sem(f"step_a{n}")
                self.step_p = sem(f"step_p{n}")
                self.start = sem(f"start{n}")
                self.staged = sem(f"q_staged{n}")
                self.product = sem(f"q_product{n}")
                self.deg = sem(f"q_deg{n}")
                self.rdeg = sem(f"q_rdeg{n}")
                self.added = sem(f"q_added{n}")
                self.bn = sem(f"q_bn{n}")
                self.stats = sem(f"q_stats{n}")
                self.std = sem(f"q_std{n}")
                self.rstd = sem(f"q_rstd{n}")
                self.factors = sem(f"q_factors{n}")
                self.norm = sem(f"q_norm{n}")
                self.zeroed = sem(f"q_zeroed{n}")
                self.stored = sem(f"q_stored{n}")
                self.all = range(self.step_v.num, self.stored.num + 1)

        def gather_groups(pool, w, table):
            with pool.Fori(0, bodies) as i:
                for u in range(UNROLL):
                    s = u % SLOTS
                    pool.wait_ge(w.idx_ready, i * UNROLL + u + 1)
                    pool.sem_inc(w.turn, 1)
                    for c in range(CPG):
                        pool.indirect_dma_start(
                            out=rows[:, s, c, :], out_offset=None, in_=table,
                            in_offset=bass.IndirectOffsetOnAxis(ap=idx[:, s, c:c + 1], axis=0)).then_inc(w.gathered[s], 16)

        def forget_gathers(pool, w):
            for s in range(SLOTS):
                pool.wait_ge(w.gathered[s], groups // SLOTS * 16 * CPG)
            pool.dma_reset(range(w.gathered[0].num, w.gathered[-1].num + 1))

        def stage_first_indices(w):
            for s in range(SLOTS):
                nc.scalar.copy(idx[:, s, :], src_t[:, s * CPG:(s + 1) * CPG]).then_inc(w.idx_ready, 1)

        def stage_indices(w, i, u):
            nc.scalar.copy(idx[:, u % SLOTS, :],
                           src_t[:, bass.ds((i * UNROLL + u + SLOTS) * CPG, CPG)]).then_inc(w.idx_ready, 1)

        def rows_in(pe, w, i, u):
            pe.wait_ge(w.gathered[u % SLOTS], (i * (UNROLL // SLOTS) + u // SLOTS + 1) * 16 * CPG)

        def make_onehot(i, u):
            r = rel_t[:, bass.ds((i * UNROLL + u) * CPG, CPG)]
            return nc.vector.tensor_tensor(oh1[:, u % 2], r.unsqueeze(2).to_broadcast([P, CPG, WIN]),
                                           lane[:, :].unsqueeze(1).to_broadcast([P, CPG, WIN]), ALU.is_equal)

        def add_group(dve, w, i, u, ready, sums, kinds):
            _, starts = nc.values_load_multi_w_load_instructions(
                base[0:1, bass.ds((i * UNROLL + u) * CPG, CPG)], engines=DVE_ONLY, min_val=0, max_val=n_nodes,
                skip_runtime_bounds_check_because="clamped to the number of nodes, and acc is padded")
            dve.wait_ge(ready, i * UNROLL + u + 1 + 2)
            dve.wait_ge(w.group_added, i * UNROLL + u + 2)
            for c in range(CPG):
                target = acc[:, 0:kinds, bass.ds(starts[c], WIN)]
                if c:
                    dve.wait_ge(w.rmw, i * (UNROLL * (CPG - 1)) + u * (CPG - 1) + c)
                add = nc.vector.tensor_tensor(target, target, sums[:, :, c, :], ALU.add)
                add.then_inc(w.rmw if c < CPG - 1 else w.group_added, 1)

        def next_sweep(dve, w):
            nc.vector.tensor_scalar(lane[:, :], lane[:, :], float(WIN), None, ALU.add).then_inc(w.moved, 1)
            nc.vector.memset(gate[:, :], 0.0).then_inc(w.moved, 1)
            nc.vector.tensor_scalar(base[0:1, :], base[0:1, :], float(WIN), float(n_nodes), ALU.add,
                                    ALU.min).then_inc(w.moved, 1)
            dve.wait_ge(w.moved, 3)

        def load_relations_by_body(sp, w):
            def relations(i, h, count):
                for q in range(count):
                    g0 = (i * UNROLL + h * HALF + q) * group_edges
                    one = etype[g0:g0 + group_edges] if isinstance(g0, int) else etype[bass.ds(g0, group_edges)]
                    sp.dma_start(erep[:, h, q, :],
                                 one.rearrange("(c e) -> c e", c=CPG).unsqueeze(1).to_broadcast([CPG, n_rels, P])
                                 ).then_inc(w.relations_in[h], 16)

            def last_half():
                e0 = full_chunks * P
                part = last_group_chunks * n_rels
                sp.dma_start(erep[part:part + n_rels, 1, HALF - 1, 0:rest_edges],
                             etype[e0:n_edges].rearrange("(c e) -> c e", c=1).to_broadcast([n_rels, rest_edges])
                             ).then_inc(w.relations_tail, 16)
                sp.wait_ge(w.relations_tail, 16)
                relations(bodies - 1, 1, HALF - 1)
                g0 = last_group * group_edges
                sp.dma_start(erep[0:part, 1, HALF - 1, :],
                             etype[g0:e0].rearrange("(c e) -> c e", e=P).unsqueeze(1)
                             .to_broadcast([last_group_chunks, n_rels, P])).then_inc(w.relations_in[1], 16)

            def load(i):
                first = isinstance(i, int) and i == 0
                last = isinstance(i, int) and i == bodies - 1
                for h in range(2):
                    if not first:
                        sp.wait_ge(w.eoh_ready, i * 2 + h - 1)
                    if last and h:
                        last_half()
                    else:
                        relations(i, h, HALF)

            return load

        def copy_sums(act, w, i, u):
            act.wait_ge(w.y_done, i * UNROLL + u + 1)
            act.wait_ge(w.z_done, i * UNROLL + u + 1 + 2)
            nc.scalar.copy(zsb[:, u % 2], zps[u % 2][:, :, :, :]).then_inc(w.z_copied, 1)
            stage_indices(w, i, u)

        def scale_onehot(dve, w, i, u):
            g = i * UNROLL + u
            h = u // HALF
            if u % HALF == 0:
                dve.wait_ge(w.wc_ready, i * 2 + h + 1)
                dve.wait_ge(w.relations_in[h], (i + 1) * 16 * HALF)
                nc.vector.tensor_scalar(eoh[:, h], erep[:, h], rel_of_p[:, 0:1], None,
                                        ALU.is_equal).then_inc(w.eoh_ready, 1)
            make_onehot(i, u).then_inc(w.onehot, 1)
            dve.wait_ge(w.z_done, g + 1)
            dve.wait_ge(w.wc_ready, i * 2 + h + 1 + 2)
            dve.wait_ge(w.onehot, g + 1)
            nc.vector.tensor_tensor(
                a[:, u % 2], oh1[:, u % 2].unsqueeze(2).to_broadcast([P, CPG, n_bases, WIN]),
                wcp[:, h, u % HALF, :].rearrange("p (c b) -> p c b", c=CPG).unsqueeze(3)
                .to_broadcast([P, CPG, n_bases, WIN]), ALU.mult).then_inc(w.a_ready, 1)

        def basis_sums(pe, w, i, u):
            g = i * UNROLL + u
            h = u // HALF
            if u % HALF == 0:
                pe.wait_ge(w.a_ready, g + 1)
                pe.wait_ge(w.eoh_ready, i * 2 + h + 1)
                for q in range(HALF):
                    last = nc.tensor.matmul(wcp[:, h, q, :], eoh[:, h, q, :],
                                            wc_blk[:, :, :].rearrange("p c b -> p (c b)"), start=True, stop=True)
                last.then_inc(w.wc_ready, 1)
            pe.wait_ge(w.z_copied, g + 1)
            pe.wait_ge(w.a_ready, g + 1 + 1)
            rows_in(pe, w, i, u)
            for c in range(CPG):
                last = nc.tensor.matmul(zps[u % 2][:, c], rows[:, u % SLOTS, c, :], a[:, u % 2, c],
                                        start=True, stop=True)
            last.then_inc(w.z_done, 1)

        def project(pe, w, i, u):
            g = i * UNROLL + u
            pe.wait_ge(w.group_added, g + 1)
            pe.wait_ge(w.z_copied, g + 1 + 2)
            for b in range(n_bases):
                last = nc.tensor.matmul(yps[u % 2][:, 0], wb[:, b, :], zsb[:, u % 2, :, b, :],
                                        start=(b == 0), stop=(b == n_bases - 1))
            last.then_inc(w.y_done, 1)

        def turn_x1(pe, w, i):
            pe.wait_ge(w.xt_ready, i + 1)
            pe.wait_ge(w.staged, i + 1)
            for j in range(TPH):
                last = nc.tensor.transpose(tps[0][:, j, :], stage[:, 0, j, :], ident[:, :])
            last.then_inc(w.turned, 1)

        def self_product(pe, w, i):
            pe.wait_ge(w.self_added, i + 1)
            pe.wait_ge(w.xt_ready, i + 1 + 1)
            for j in range(TPH):
                nc.tensor.matmul(tps[1][:, j, :], xt[:, j, :], ws[:, :], start=True, stop=False)
                last = nc.tensor.matmul(tps[1][:, j, :], onesm[0:1, :], bself[0:1, :], start=False, stop=True)
            last.then_inc(w.self_done, 1)

        def stage_x1(act, w, i):
            act.wait_ge(w.turned, i + 1)
            nc.scalar.copy(stage[:, 0], nodes[:, bass.ds(i * TPH, TPH), :]).then_inc(w.staged, 1)

        def copy_x1t(act, w, i):
            act.wait_ge(w.self_done, i + 1)
            act.wait_ge(w.turned, i + 1 + 1)
            nc.scalar.copy(xt[:, :, :], tps[0][:, :, :]).then_inc(w.xt_ready, 1)

        def free_slot(act, w, i, u):
            act.wait_ge(w.z_done, i * UNROLL + u + 1 + 2)
            stage_indices(w, i, u)

        def plain_onehot(dve, w, i, u):
            dve.wait_ge(w.z_done, i * UNROLL + u + 1)
            make_onehot(i, u).then_inc(w.a_ready, 1)

        def add_self(dve, w, i):
            four = nodes[:, bass.ds(i * TPH, TPH), :]
            dve.wait_ge(w.self_done, i + 1 + 1)
            nc.vector.scalar_tensor_tensor(out=four, in0=tps[1][:, :, :], scalar=gate[:, 0:1], in1=four,
                                           op0=ALU.mult, op1=ALU.add).then_inc(w.self_added, 1)

        def plain_sums(pe, w, i, u):
            g = i * UNROLL + u
            pe.wait_ge(w.group_added, g + 1)
            pe.wait_ge(w.a_ready, g + 1)
            nc.tensor.matmul(yps[u % 2][:, 1], onesm[:, :], oh1[:, u % 2], start=True, stop=True)
            rows_in(pe, w, i, u)
            for c in range(CPG):
                last = nc.tensor.matmul(yps[u % 2][:, 0, c], rows[:, u % SLOTS, c, :], oh1[:, u % 2, c],
                                        start=True, stop=True)
            last.then_inc(w.z_done, 1)

        def stage_sums(act, n, k, st, fresh=False):
            if not fresh:
                act.wait_ge(n.product, k + 1)
            nc.scalar.copy(stage[:, st], acc[:, 0, bass.ds(k * QUAD, QUAD)]).then_inc(n.staged, 1)

        def stage_sums_and_degrees(act, n, k, st, fresh=False):
            if not fresh:
                act.wait_ge(n.product, k + 1)
            nc.scalar.copy(deg_st[0:1, st], acc[0:1, 1, bass.ds(k * QUAD, QUAD)])
            nc.scalar.copy(stage[:, st], acc[:, 0, bass.ds(k * QUAD, QUAD)]).then_inc(n.staged, 1)

        def turn_sums(pe, n, k, st, bank, fresh=False):
            if not fresh:
                pe.wait_ge(n.added, k + 1)
            pe.wait_ge(n.staged, k + 1)
            for j in range(TPH):
                last = nc.tensor.transpose(bank[:, j, :], stage[:, st, j, :], ident[:, :])
            last.then_inc(n.product, 1)

        def neigh_product(pe, n, k, st, bank, dbank, fresh=False):
            if not fresh:
                pe.wait_ge(n.added, k + 1)
            pe.wait_ge(n.staged, k + 1)
            for j in range(TPH):
                nc.tensor.matmul(dbank[:, j:j + 1], deg_st[0:1, st, j, :], onesm[0:1, 0:1], start=True, stop=True)
            for j in range(TPH):
                last = nc.tensor.matmul(bank[:, j, :], stage[:, st, j, :], wn[:, :], start=True, stop=True)
            last.then_inc(n.product, 1)

        def add_sums(dve, n, k, bank):
            four = nodes[:, bass.ds(k * TPH, TPH), :]
            dve.wait_ge(n.product, k + 1 + n.depth)
            nc.vector.tensor_tensor(four, four, bank, ALU.add).then_inc(n.added, 1)

        def add_mean(dve, n, k, h, bank, dbank):
            dve.wait_ge(n.product, k + 1 + n.depth)
            nc.vector.tensor_scalar(rdeg[:, h, :], dbank[:, 0:TPH], 1.0, None, ALU.max).then_inc(n.deg, 1)
            dve.wait_ge(n.deg, k + 1)
            nc.vector.reciprocal(rdeg[:, h, :], rdeg[:, h, :]).then_inc(n.rdeg, 1)
            dve.wait_ge(n.rdeg, k + 1)
            for j in range(TPH):
                t = nodes[:, bass.ds(k * TPH + j, 1), :].rearrange("p o f -> p (o f)")
                last = nc.vector.scalar_tensor_tensor(out=t, in0=bank[:, j, :], scalar=rdeg[:, h, j:j + 1],
                                                      in1=t, op0=ALU.mult, op1=ALU.add)
            last.then_inc(n.added, 1)

        def tile_stats(dve, n, k, h):
            dve.wait_ge(n.added, k + 1 + n.depth)
            dve.sem_inc(n.step_v, 1)
            for j in range(TPH):
                last = nc.vector.bn_stats(stats[:, h, j, :], nodes[:, bass.ds(k * TPH + j, 1), :])
            last.then_inc(n.bn, 1)
            dve.wait_ge(n.bn, k + 1)
            dve.sem_inc(n.step_v, 1)
            for j in range(TPH):
                last = nc.vector.bn_aggr(mv[:, h, j, :], stats[:, h, j, :])
            last.then_inc(n.stats, 1)

        def roots(act, n, k, h):
            act.wait_ge(n.stats, k + 1)
            nc.scalar.activation(std[:, h, :], mv[:, h, :, 1], ACT.Sqrt, bias=epst[:, 0:1],
                                 scale=1.0).then_inc(n.std, 1)

        def tile_factors(dve, n, k, h, fresh=False):
            if not fresh:
                dve.wait_ge(n.norm, k + 1)
            dve.wait_ge(n.std, k + 1)
            nc.vector.reciprocal(rstd[:, h, :], std[:, h, :]).then_inc(n.rstd, 1)
            dve.wait_ge(n.rstd, k + 1)
            nc.vector.scalar_tensor_tensor(out=shift[:, h, :], in0=mv[:, h, :, 0], scalar=-1.0, in1=rstd[:, h, :],
                                           op0=ALU.mult, op1=ALU.mult).then_inc(n.factors, 1)

        def normalise(act, n, k, h):
            act.wait_ge(n.factors, k + 1)
            act.sem_inc(n.step_a, 1)
            for j in range(TPH):
                t = nodes[:, bass.ds(k * TPH + j, 1), :]
                last = nc.scalar.activation(t, t, ACT.Identity, bias=shift[:, h, j:j + 1], scale=rstd[:, h, j:j + 1])
            last.then_inc(n.norm, 1)

        def store_x1(sp, n, k):
            sp.wait_ge(n.norm, k + 1 + n.depth)
            sp.dma_start(x1_rows[bass.ds(k * QUAD, QUAD), :].rearrange("(t p) f -> p t f", p=P),
                         nodes[:, bass.ds(k * TPH, TPH), :]).then_inc(n.stored, 16)

        def store_out(sp, n, k):
            sp.wait_ge(n.norm, k + 1 + n.depth)
            sp.dma_start(out[bass.ds(k * QUAD, QUAD), :].rearrange("(t p) f -> p t f", p=P),
                         nodes[:, bass.ds(k * TPH, TPH), :]).then_inc(n.stored, 16)

        real_quads = -(-ntiles // TPH)
        whole = n_nodes // QUAD
        assert whole == real_quads - 1 and full_ntiles == whole * TPH + 1

        def store_last_out(sp, n):
            sp.wait_ge(n.norm, whole + 1 + n.depth)
            sp.dma_start(out[whole * QUAD:full_ntiles * P, :], nodes[:, full_ntiles - 1, :]).then_inc(n.stored, 16)
            sp.dma_start(out[full_ntiles * P:n_nodes, :], nodes[0:rest_nodes, full_ntiles, :]).then_inc(n.stored, 16)
            sp.wait_ge(n.stored, (whole + 2) * 16)

        fbank = [zbanks[b][:, 0] for b in range(2)]
        dbank = [zbanks[b][:, 1, 0] for b in range(2)]

        with nc.If(in_order):
            w1, w2 = Sweep("_o1"), Sweep("_o2")
            n1, n2 = Norm("_o1", 1), Norm("_o2", 1)
            acc_set = [sem(f"acc_set{n}") for n in range(2)]
            late_quads = list(range(bodies - LAG, real_quads))
            assert len(late_quads) == 2
            with nc.Block() as block:
                @block.sync
                def _(sp):
                    load = load_relations_by_body(sp, w1)
                    for i in range(LAG):
                        load(i)
                    with sp.Fori(LAG, bodies - 1) as i:
                        load(i)
                        store_x1(sp, n1, i - LAG)
                    load(bodies - 1)
                    store_x1(sp, n1, bodies - 1 - LAG)
                    for k in late_quads:
                        store_x1(sp, n1, k)
                    with sp.Fori(LAG, bodies) as i:
                        store_out(sp, n2, i - LAG)
                    for k in late_quads[:-1]:
                        store_out(sp, n2, k)
                    store_last_out(sp, n2)

                @block.gpsimd
                def _(pool):
                    gather_groups(pool, w1, x_in)
                    pool.wait_ge(n1.stored, real_quads * 16)
                    pool.sem_inc(w1.turn, 1)
                    gather_groups(pool, w2, x1_rows[0:n_nodes, :])

                @block.scalar
                def _(act):
                    act.sem_inc(w1.z_copied, 2)
                    act.sem_inc(n1.norm, 1)
                    stage_first_indices(w1)
                    nc.scalar.copy(acc[:, 0, :], bias_col[:, 0:1].to_broadcast([P, nodes_p])).then_inc(acc_set[0], 1)
                    with act.Fori(0, LAG) as i:
                        for u in range(UNROLL):
                            copy_sums(act, w1, i, u)
                    with act.Fori(LAG, bodies) as i:
                        k = i - LAG
                        for u in range(UNROLL):
                            copy_sums(act, w1, i, u)
                            if u == 0:
                                act.wait_ge(w1.group_added, i * UNROLL + 2)
                                stage_sums(act, n1, k, 0)
                            if u == 3:
                                roots(act, n1, k, 0)
                            if u == 5:
                                normalise(act, n1, k, 0)
                    act.wait_ge(w1.group_added, groups + 2)
                    for h, k in enumerate(late_quads):
                        stage_sums(act, n1, k, h, fresh=(h == 1))
                    for h, k in enumerate(late_quads):
                        roots(act, n1, k, h)
                    for h, k in enumerate(late_quads):
                        normalise(act, n1, k, h)

                    act.sem_inc(w2.xt_ready, 1)
                    act.sem_inc(n2.norm, 1)
                    stage_first_indices(w2)
                    act.wait_ge(n1.norm, real_quads + 1)
                    act.sem_inc(n1.start, 1)

                    def layer2(i, quads_too):
                        k = i - LAG
                        for u in range(UNROLL):
                            if u == 0:
                                stage_x1(act, w2, i)
                            if u == 1 and quads_too:
                                act.wait_ge(w2.group_added, i * UNROLL + 2)
                                stage_sums_and_degrees(act, n2, k, 1)
                            if u == 3:
                                copy_x1t(act, w2, i)
                            if u == 4 and quads_too:
                                roots(act, n2, k, 0)
                            if u == 6 and quads_too:
                                normalise(act, n2, k, 0)
                            free_slot(act, w2, i, u)

                    with act.Fori(0, LAG) as i:
                        layer2(i, False)
                    with act.Fori(LAG, bodies) as i:
                        layer2(i, True)
                    act.wait_ge(w2.group_added, groups + 2)
                    act.wait_ge(w2.turned, bodies + 1)
                    act.sem_inc(n1.start, 1)
                    for h, k in enumerate(late_quads):
                        stage_sums_and_degrees(act, n2, k, 1 - h, fresh=(h == 1))
                    for h, k in enumerate(late_quads):
                        roots(act, n2, k, h)
                    for h, k in enumerate(late_quads):
                        normalise(act, n2, k, h)

                @block.vector
                def _(dve):
                    dve.sem_inc(w1.a_ready, 1)
                    dve.sem_inc(w1.group_added, 2)
                    dve.sem_inc(n1.added, 1)

                    def zero_quad(k):
                        nc.vector.tensor_copy(acc[:, 0, bass.ds(k * QUAD, QUAD)],
                                              zero[:, 0:1].to_broadcast([P, QUAD])).then_inc(n1.zeroed, 1)

                    def layer1(i, quads_too):
                        k = i - LAG
                        for u in range(UNROLL):
                            scale_onehot(dve, w1, i, u)
                            if u >= 2:
                                add_group(dve, w1, i, u - 2, w1.y_done, yps[u % 2][:, 0:1], 1)
                            if u == 2 and quads_too:
                                add_sums(dve, n1, k, tps[1][:, :, :])
                                zero_quad(k)
                                tile_stats(dve, n1, k, 0)
                            if u == 4 and quads_too:
                                tile_factors(dve, n1, k, 0)
                        for u in (UNROLL - 2, UNROLL - 1):
                            add_group(dve, w1, i, u, w1.y_done, yps[u % 2][:, 0:1], 1)

                    dve.wait_ge(acc_set[0], 1)
                    dve.wait_ge(s_x, 32)
                    dve.sem_inc(n1.start, 1)
                    with dve.Fori(0, LAG) as i:
                        layer1(i, False)
                    with dve.Fori(LAG, bodies) as i:
                        layer1(i, True)
                    for h, k in enumerate(late_quads):
                        add_sums(dve, n1, k, tps[1 - h][:, :, :])
                        zero_quad(k)
                        tile_stats(dve, n1, k, h)
                    for h, k in enumerate(late_quads):
                        tile_factors(dve, n1, k, h, fresh=(h == 1))

                    nc.vector.memset(acc[:, 1, :], 0.0).then_inc(acc_set[1], 1)
                    dve.wait_ge(acc_set[1], 1)
                    dve.wait_ge(n1.norm, real_quads + 1)
                    dve.sem_inc(w2.group_added, 2)
                    dve.sem_inc(w2.self_added, 1)
                    dve.sem_inc(n2.added, 1)

                    def layer2(i, quads_too):
                        k = i - LAG
                        for u in range(UNROLL):
                            plain_onehot(dve, w2, i, u)
                            if u == 6:
                                add_self(dve, w2, i)
                            if u >= 2:
                                add_group(dve, w2, i, u - 2, w2.z_done, yps[u % 2], 2)
                            if u == 3 and quads_too:
                                add_mean(dve, n2, k, 0, fbank[0], dbank[0])
                                tile_stats(dve, n2, k, 0)
                            if u == 5 and quads_too:
                                tile_factors(dve, n2, k, 0)
                        for u in (UNROLL - 2, UNROLL - 1):
                            add_group(dve, w2, i, u, w2.z_done, yps[u % 2], 2)

                    with dve.Fori(0, LAG) as i:
                        layer2(i, False)
                    with dve.Fori(LAG, bodies) as i:
                        layer2(i, True)
                    for h, k in enumerate(late_quads):
                        add_mean(dve, n2, k, h, fbank[h], dbank[h])
                        tile_stats(dve, n2, k, h)
                    for h, k in enumerate(late_quads):
                        tile_factors(dve, n2, k, h, fresh=(h == 1))

                @block.tensor
                def _(pe):
                    pe.sem_inc(w1.wc_ready, 2)
                    pe.sem_inc(w1.z_done, 2)
                    pe.sem_inc(w1.y_done, 2)
                    pe.sem_inc(n1.product, 1)

                    def layer1(i, quads_too):
                        for u in range(UNROLL):
                            basis_sums(pe, w1, i, u)
                            if u == 1 and quads_too:
                                turn_sums(pe, n1, i - LAG, 0, tps[1])
                            if u:
                                project(pe, w1, i, u - 1)
                        project(pe, w1, i, UNROLL - 1)

                    with pe.Fori(0, LAG) as i:
                        layer1(i, False)
                    with pe.Fori(LAG, bodies) as i:
                        layer1(i, True)
                    for h, k in enumerate(late_quads):
                        turn_sums(pe, n1, k, h, tps[1 - h], fresh=(h == 1))

                    pe.wait_ge(n1.added, real_quads + 1)
                    pe.sem_inc(w2.z_done, 2)
                    pe.sem_inc(w2.turned, 1)
                    pe.sem_inc(w2.self_done, 1)
                    pe.sem_inc(n2.product, 1)

                    def layer2(i, quads_too):
                        for u in range(UNROLL):
                            plain_sums(pe, w2, i, u)
                            if u == 1:
                                turn_x1(pe, w2, i)
                            if u == 2 and quads_too:
                                neigh_product(pe, n2, i - LAG, 1, fbank[0], dbank[0])
                            if u == 4:
                                self_product(pe, w2, i)

                    with pe.Fori(0, LAG) as i:
                        layer2(i, False)
                    with pe.Fori(LAG, bodies) as i:
                        layer2(i, True)
                    for h, k in enumerate(late_quads):
                        neigh_product(pe, n2, k, 1 - h, fbank[h], dbank[h], fresh=(h == 1))

        with nc.Else():
            w = Sweep("_a")
            n = Norm("_a", 2)
            base_kept = sem("base_kept")
            with nc.Block() as block:
                @block.scalar
                def _(act):
                    nc.scalar.copy(acc[:, 0, :], bias_col[:, 0:1].to_broadcast([P, nodes_p])).then_inc(base_kept, 1)
                    act.wait_ge(base_kept, 1)

                @block.vector
                def _(dve):
                    nc.vector.tensor_copy(base0[0:1, :], base[0:1, :]).then_inc(base_kept, 1)
                    dve.wait_ge(base_kept, 1)
                    dve.wait_ge(s_x, 32)

            nc.all_engine_barrier()

            with nc.Fori(0, span_v + 1, WIN):
                with nc.Block() as block:
                    @block.sync
                    def _(sp):
                        load = load_relations_by_body(sp, w)
                        load(0)
                        with sp.Fori(1, bodies - 1) as i:
                            load(i)
                        load(bodies - 1)

                    @block.gpsimd
                    def _(pool):
                        gather_groups(pool, w, x_in)
                        forget_gathers(pool, w)

                    @block.scalar
                    def _(act):
                        act.sem_inc(w.z_copied, 2)
                        stage_first_indices(w)
                        with act.Fori(0, bodies) as i:
                            for u in range(UNROLL):
                                copy_sums(act, w, i, u)

                    @block.vector
                    def _(dve):
                        dve.sem_inc(w.a_ready, 1)
                        dve.sem_inc(w.group_added, 2)
                        with dve.Fori(0, bodies) as i:
                            for u in range(UNROLL):
                                scale_onehot(dve, w, i, u)
                                if u >= 2:
                                    add_group(dve, w, i, u - 2, w.y_done, yps[u % 2][:, 0:1], 1)
                            for u in (UNROLL - 2, UNROLL - 1):
                                add_group(dve, w, i, u, w.y_done, yps[u % 2][:, 0:1], 1)
                        dve.wait_ge(w.group_added, groups + 2)
                        next_sweep(dve, w)

                    @block.tensor
                    def _(pe):
                        pe.sem_inc(w.wc_ready, 2)
                        pe.sem_inc(w.z_done, 2)
                        pe.sem_inc(w.y_done, 2)
                        with pe.Fori(0, bodies) as i:
                            for u in range(UNROLL):
                                basis_sums(pe, w, i, u)
                                if u:
                                    project(pe, w, i, u - 1)
                            project(pe, w, i, UNROLL - 1)

                nc.all_engine_barrier(sems_to_clear=w.all)

            with nc.Block() as block:
                @block.scalar
                def _(act):
                    act.sem_inc(n.norm, 2)
                    with act.Fori(0, nbodies) as i:
                        for h in range(2):
                            stage_sums(act, n, i * 2 + h, h)
                        for h in range(2):
                            roots(act, n, i * 2 + h, h)
                        for h in range(2):
                            normalise(act, n, i * 2 + h, h)

                @block.tensor
                def _(pe):
                    pe.sem_inc(n.product, 2)
                    with pe.Fori(0, nbodies) as i:
                        for h in range(2):
                            turn_sums(pe, n, i * 2 + h, h, tps[h])

                @block.vector
                def _(dve):
                    dve.sem_inc(n.added, 2)
                    nc.vector.tensor_copy(base[0:1, :], base0[0:1, :]).then_inc(n.start, 1)
                    nc.vector.tensor_copy(lane[:, :], lane_i[:, :])
                    nc.vector.memset(gate[:, :], 1.0)
                    with dve.Fori(0, nbodies) as i:
                        for h in range(2):
                            add_sums(dve, n, i * 2 + h, tps[h][:, :, :])
                            tile_stats(dve, n, i * 2 + h, h)
                        for h in range(2):
                            tile_factors(dve, n, i * 2 + h, h)

                @block.gpsimd
                def _(pool):
                    pool.wait_ge(n.start, 1)
                    with pool.Fori(0, nbodies) as i:
                        for h in range(2):
                            k = i * 2 + h
                            pool.wait_ge(n.staged, k + 1)
                            pool.sem_inc(n.step_p, 1)
                            nc.gpsimd.tensor_copy(acc[:, :, bass.ds(k * QUAD, QUAD)],
                                                  zero[:, 0:1].unsqueeze(2).to_broadcast([P, 2, QUAD]))

                @block.sync
                def _(sp):
                    with sp.Fori(0, nbodies) as i:
                        for h in range(2):
                            store_x1(sp, n, i * 2 + h)
                    sp.wait_ge(n.stored, bodies * 16)

            nc.all_engine_barrier(sems_to_clear=n.all)

            with nc.Fori(0, span_v + 1, WIN):
                with nc.Block() as block:
                    @block.gpsimd
                    def _(pool):
                        gather_groups(pool, w, x1_rows[0:n_nodes, :])
                        forget_gathers(pool, w)

                    @block.scalar
                    def _(act):
                        act.sem_inc(w.xt_ready, 1)
                        stage_first_indices(w)
                        with act.Fori(0, bodies) as i:
                            for u in range(UNROLL):
                                if u == 0:
                                    stage_x1(act, w, i)
                                if u == 3:
                                    copy_x1t(act, w, i)
                                free_slot(act, w, i, u)

                    @block.vector
                    def _(dve):
                        dve.sem_inc(w.group_added, 2)
                        dve.sem_inc(w.self_added, 1)
                        with dve.Fori(0, bodies) as i:
                            for u in range(UNROLL):
                                plain_onehot(dve, w, i, u)
                                if u == 6:
                                    add_self(dve, w, i)
                                if u >= 2:
                                    add_group(dve, w, i, u - 2, w.z_done, yps[u % 2], 2)
                            for u in (UNROLL - 2, UNROLL - 1):
                                add_group(dve, w, i, u, w.z_done, yps[u % 2], 2)
                        dve.wait_ge(w.group_added, groups + 2)
                        next_sweep(dve, w)

                    @block.tensor
                    def _(pe):
                        pe.sem_inc(w.z_done, 2)
                        pe.sem_inc(w.turned, 1)
                        pe.sem_inc(w.self_done, 1)
                        with pe.Fori(0, bodies) as i:
                            for u in range(UNROLL):
                                plain_sums(pe, w, i, u)
                                if u == 1:
                                    turn_x1(pe, w, i)
                                if u == 4:
                                    self_product(pe, w, i)

                nc.all_engine_barrier(sems_to_clear=w.all)

            with nc.Block() as block:
                @block.scalar
                def _(act):
                    act.sem_inc(n.norm, 2)
                    with act.Fori(0, nbodies) as i:
                        for h in range(2):
                            stage_sums_and_degrees(act, n, i * 2 + h, h)
                        for h in range(2):
                            roots(act, n, i * 2 + h, h)
                        for h in range(2):
                            normalise(act, n, i * 2 + h, h)

                @block.tensor
                def _(pe):
                    pe.sem_inc(n.product, 2)
                    with pe.Fori(0, nbodies) as i:
                        for h in range(2):
                            neigh_product(pe, n, i * 2 + h, h, fbank[h], dbank[h])

                @block.vector
                def _(dve):
                    dve.sem_inc(n.added, 2)
                    with dve.Fori(0, nbodies) as i:
                        for h in range(2):
                            add_mean(dve, n, i * 2 + h, h, fbank[h], dbank[h])
                            tile_stats(dve, n, i * 2 + h, h)
                        for h in range(2):
                            tile_factors(dve, n, i * 2 + h, h)

                @block.sync
                def _(sp):
                    with sp.Fori(0, whole // 2) as i:
                        for h in range(2):
                            store_out(sp, n, i * 2 + h)
                    store_last_out(sp, n)


_INS = ["x", "src", "dst", "edge_type_16", "L0_gnn_weight", "L0_gnn_w_comp", "L0_gnn_h_bias", "L1_gnn_W_neigh",
        "L1_gnn_W_self", "L1_gnn_b_self"]


def kernel(**inputs):
    import numpy as _np
    import concourse.bacc as _bacc
    from concourse import mybir as _mybir
    from concourse.bass_utils import run_bass_kernel_spmd as _run

    nc = _bacc.Bacc("TRN2", target_bir_lowering=False, num_devices=1)
    arrays, args = {}, []
    for name in _INS:
        a = _np.ascontiguousarray(inputs[name])
        arrays[f"in_{name}_dram"] = a
        args.append(nc.dram_tensor(f"in_{name}_dram", a.shape, _mybir.dt.from_np(a.dtype), kind="ExternalInput").ap())
    n_nodes, d = inputs["x"].shape
    step = P * UNROLL
    x1_rows = nc.dram_tensor("x1_rows", (-(-n_nodes // step) * step, d), F32, kind="Internal").ap()
    out = nc.dram_tensor("out_dram", (n_nodes, d), F32, kind="ExternalOutput").ap()
    gnn_kernel(nc, *args, x1_rows, out)
    r = _run(nc, [arrays], core_ids=[0])
    return r.results[0]["out_dram"]
```
